# Optimizing a Trainium2 kernel written in Bass

```python
import numpy as np
import jax
import jax.numpy as jnp

def _softmax(x, axis=-1):
    return jax.nn.softmax(x, axis=axis)

def _gelu(x):
    return jax.nn.gelu(x, approximate=True)

def _silu(x):
    return jax.nn.silu(x)

def _sigmoid(x):
    return jax.nn.sigmoid(x)

def _layernorm(x, axis=-1, eps=1e-05):
    m = jnp.mean(x, axis=axis, keepdims=True)
    v = jnp.var(x, axis=axis, keepdims=True)
    return (x - m) / jnp.sqrt(v + eps)

def _scatter_add(tgt, idx, src, axis=0):
    return tgt.at[idx].add(src)

def _segment_sum(src, seg, n):
    return jax.ops.segment_sum(src, seg, n)
kernel_name = 'mk_seq_postln_d1_jaxref_r8_98d79b'

def setup_inputs(seed: int=0):
    np.random.seed(seed)
    _w = jnp.asarray

    def _L0_attn_setup():
        import jax, jax.numpy as jnp
        import numpy as np
        NUM_HEADS = 16

        def _sinusoid_rel_pos(seq_len, dim):
            pos = jnp.arange(seq_len - 1, -1, -1, dtype=jnp.float32)
            inv_freq = 1.0 / 10000.0 ** (jnp.arange(0, dim, 2, dtype=jnp.float32) / dim)
            ang = pos[:, None] * inv_freq[None, :]
            return jnp.concatenate([jnp.sin(ang), jnp.cos(ang)], axis=-1)

        def _rel_shift(x):
            B, H, S, L = x.shape
            x = jnp.pad(x, ((0, 0), (0, 0), (0, 0), (1, 0)))
            x = x.reshape(B, H, L + 1, S)
            return x[:, :, 1:S + 1, :]
        key = jax.random.key(seed)
        ks = jax.random.split(key, 8)
        B, S, C = (2, 256, 128)
        Dk, Dv, H = (128, 128, NUM_HEADS)
        dk = Dk // H
        scale = 0.02
        return {'x': jax.random.normal(ks[0], (B, S, C), dtype=jnp.float32), 'Wq': jax.random.normal(ks[1], (C, Dk), dtype=jnp.float32) * scale, 'Wk': jax.random.normal(ks[2], (C, Dk), dtype=jnp.float32) * scale, 'Wv': jax.random.normal(ks[3], (C, Dv), dtype=jnp.float32) * scale, 'u': jax.random.normal(ks[4], (H, dk), dtype=jnp.float32) * scale, 'v': jax.random.normal(ks[5], (H, dk), dtype=jnp.float32) * scale, 'Wo': jax.random.normal(ks[6], (Dv, C), dtype=jnp.float32) * scale, 'bo': jnp.zeros((C,), dtype=jnp.float32)}
    _L0_attn_in = _L0_attn_setup()

    def _L0_ffn_setup():
        import jax, jax.numpy as jnp
        import numpy as np
        BLOCK = 16
        _GRID = jnp.array([0.0, 0.5, 1.0, 1.5, 2.0, 3.0, 4.0, 6.0], dtype=jnp.float32)
        _MID = jnp.array([0.25, 0.75, 1.25, 1.75, 2.5, 3.5, 5.0], dtype=jnp.float32)

        def fp4_quant_dequant(x):
            shape = x.shape
            xb = x.reshape(shape[:-1] + (shape[-1] // BLOCK, BLOCK))
            scale = jnp.max(jnp.abs(xb), axis=-1, keepdims=True) / 6.0
            scale = jnp.maximum(scale, jnp.float32(1e-12))
            xn = xb / scale
            idx = jnp.searchsorted(_MID, jnp.abs(xn))
            q = _GRID[idx] * jnp.sign(xn) * scale
            return q.reshape(shape)

        def fp4_linear(x, w):
            xq = fp4_quant_dequant(x)
            wq = fp4_quant_dequant(w)
            return jnp.einsum('bsk,nk->bsn', xq, wq)
        key = jax.random.key(seed)
        k1, k2, k3, k4 = jax.random.split(key, 4)
        H, I = (128, 352)
        x = jax.random.normal(k1, (4, 512, H), dtype=jnp.float32)
        w_gate = jax.random.normal(k2, (I, H), dtype=jnp.float32) * 0.02
        w_up = jax.random.normal(k3, (I, H), dtype=jnp.float32) * 0.02
        w_down = jax.random.normal(k4, (H, I), dtype=jnp.float32) * 0.02
        return {'x': x, 'w_gate': w_gate, 'w_up': w_up, 'w_down': w_down}
    _L0_ffn_in = _L0_ffn_setup()
    _d = {'L0_attn_x': _L0_attn_in['x'], 'L0_attn_Wq': _L0_attn_in['Wq'], 'L0_attn_Wk': _L0_attn_in['Wk'], 'L0_attn_Wv': _L0_attn_in['Wv'], 'L0_attn_u': _L0_attn_in['u'], 'L0_attn_v': _L0_attn_in['v'], 'L0_attn_Wo': _L0_attn_in['Wo'], 'L0_attn_bo': _L0_attn_in['bo'], 'L0_ffn_w_gate': _L0_ffn_in['w_gate'], 'L0_ffn_w_up': _L0_ffn_in['w_up'], 'L0_ffn_w_down': _L0_ffn_in['w_down']}
    _x0 = _d['L0_attn_x']
    _d['L0_attn_x'] = jax.random.normal(jax.random.fold_in(jax.random.key(seed), 1), (1, 2048, 128), dtype=_x0.dtype)
    del _x0
    return _d

def reference(L0_attn_x, L0_attn_Wq, L0_attn_Wk, L0_attn_Wv, L0_attn_u, L0_attn_v, L0_attn_Wo, L0_attn_bo, L0_ffn_w_gate, L0_ffn_w_up, L0_ffn_w_down):

    def _L0_attn_ref(x, Wq, Wk, Wv, u, v, Wo, bo):
        import jax, jax.numpy as jnp
        import numpy as np
        NUM_HEADS = 16

        def _sinusoid_rel_pos(seq_len, dim):
            pos = jnp.arange(seq_len - 1, -1, -1, dtype=jnp.float32)
            inv_freq = 1.0 / 10000.0 ** (jnp.arange(0, dim, 2, dtype=jnp.float32) / dim)
            ang = pos[:, None] * inv_freq[None, :]
            return jnp.concatenate([jnp.sin(ang), jnp.cos(ang)], axis=-1)

        def _rel_shift(x):
            B, H, S, L = x.shape
            x = jnp.pad(x, ((0, 0), (0, 0), (0, 0), (1, 0)))
            x = x.reshape(B, H, L + 1, S)
            return x[:, :, 1:S + 1, :]
        B, S, C = x.shape
        H = NUM_HEADS
        dk = Wq.shape[1] // H
        dv = Wv.shape[1] // H
        Q = (x @ Wq).reshape(B, S, H, dk).transpose(0, 2, 1, 3)
        K = (x @ Wk).reshape(B, S, H, dk).transpose(0, 2, 1, 3)
        V = (x @ Wv).reshape(B, S, H, dv).transpose(0, 2, 1, 3)
        r = _sinusoid_rel_pos(S, dk)
        term1 = jnp.einsum('bhqd,bhkd->bhqk', Q, K)
        term2 = jnp.einsum('bhqd,kd->bhqk', Q, r)
        term3 = jnp.einsum('hd,bhkd->bhk', u, K)[:, :, None, :]
        term4 = jnp.einsum('hd,kd->hk', v, r)[None, :, None, :]
        scores = (term1 + term3 + _rel_shift(term2 + term4)) / jnp.sqrt(jnp.asarray(dk, dtype=x.dtype))
        attn = jax.nn.softmax(scores, axis=-1)
        out = jnp.einsum('bhqk,bhkd->bqhd', attn, V).reshape(B, S, H * dv)
        return out @ Wo + bo

    def _L0_ffn_ref(x, w_gate, w_up, w_down):
        import jax, jax.numpy as jnp
        import numpy as np
        BLOCK = 16
        _GRID = jnp.array([0.0, 0.5, 1.0, 1.5, 2.0, 3.0, 4.0, 6.0], dtype=jnp.float32)
        _MID = jnp.array([0.25, 0.75, 1.25, 1.75, 2.5, 3.5, 5.0], dtype=jnp.float32)

        def fp4_quant_dequant(x):
            shape = x.shape
            xb = x.reshape(shape[:-1] + (shape[-1] // BLOCK, BLOCK))
            scale = jnp.max(jnp.abs(xb), axis=-1, keepdims=True) / 6.0
            scale = jnp.maximum(scale, jnp.float32(1e-12))
            xn = xb / scale
            idx = jnp.searchsorted(_MID, jnp.abs(xn))
            q = _GRID[idx] * jnp.sign(xn) * scale
            return q.reshape(shape)

        def fp4_linear(x, w):
            xq = fp4_quant_dequant(x)
            wq = fp4_quant_dequant(w)
            return jnp.einsum('bsk,nk->bsn', xq, wq)
        gate = fp4_linear(x, w_gate)
        y = fp4_linear(x, w_up)
        h = jax.nn.silu(gate) * y
        return fp4_linear(h, w_down)
    x = L0_attn_x
    x = _layernorm(x + _L0_attn_ref(x, L0_attn_Wq, L0_attn_Wk, L0_attn_Wv, L0_attn_u, L0_attn_v, L0_attn_Wo, L0_attn_bo), axis=-1)
    x = _layernorm(x + _L0_ffn_ref(x, L0_ffn_w_gate, L0_ffn_w_up, L0_ffn_w_down), axis=-1)
    return x

_drawn_inputs = setup_inputs


def setup_inputs(seed=0):
    import zlib

    import numpy as np

    out = dict(_drawn_inputs(seed))
    spreads = {'L0_attn_bo': (0.0, 0.1)}
    factors = {'L0_attn_Wq': 8.0,
     'L0_attn_Wk': 8.0,
     'L0_attn_Wv': 8.0,
     'L0_attn_u': 8.0,
     'L0_attn_v': 8.0,
     'L0_attn_Wo': 8.0,
     'L0_ffn_w_gate': 5.563,
     'L0_ffn_w_up': 5.313,
     'L0_ffn_w_down': 5.314}
    for name, (base, spread) in spreads.items():
        noise = np.random.default_rng([zlib.crc32(name.encode()), seed]).standard_normal(out[name].shape)
        drawn = base * np.exp(spread * noise) if base else spread * noise
        out[name] = jnp.asarray(drawn.astype(out[name].dtype))
    for name, factor in factors.items():
        out[name] = (out[name] * factor).astype(out[name].dtype)
    return out
```

```python
from contextlib import ExitStack

import numpy as np

import concourse.bass as bass
from concourse import mybir

ALU = mybir.AluOpType
ACT = mybir.ActivationFunctionType
AX = mybir.AxisListType
F32 = mybir.dt.float32
BF16 = mybir.dt.bfloat16

S, C, H = 2048, 128, 16
DK = C // H
T = S // 128
INNER = 352
SCALE = float(DK) ** -0.5
NEG = -1.0e30
LN_EPS = 1e-5

COMBOS = 6
TYPE_ROWS = COMBOS * DK
SCORE_ROWS = 2 * TYPE_ROWS
SHIFT_ROW = SCORE_ROWS
STACK_ROWS = SHIFT_ROW + 2
Q_RUNS = [(0, 0, 3), (3, 1, 2), (5, 2, 1)]
K_RUNS = [(0, 3), (3, 2), (5, 1)]
STACK_DMAS = 4 * len(Q_RUNS) + len(K_RUNS)

RING = 3
STEPS = T + 1
LEAD = STEPS + 3
ALL_STEPS = H * STEPS
BODY = RING * STEPS
TURNS = 4
SLOTS = 2
ECOLS = 512


def constants():
    bf = mybir.dt.np(BF16)
    w = 1.0 / 10000.0 ** (np.arange(0, DK, 2, dtype=np.float64) / DK)
    pos = np.arange(S, dtype=np.float64)

    def rotation(at):
        s, c = np.sin(at[None, :] * w[:, None]), np.cos(at[None, :] * w[:, None])
        return np.concatenate([s, s]), np.concatenate([c, -c])

    own_a, swap_a = rotation(pos)
    own_b, swap_b = rotation(pos + S)
    tables = np.stack([own_a, swap_a, own_b, swap_b]).astype(np.float32)
    key = np.concatenate([np.cos(pos * w[:, None]), np.sin(pos * w[:, None])]).astype(np.float32)
    hi = key.astype(bf)
    mid = (key - hi.astype(np.float32)).astype(bf)
    lo = (key - hi.astype(np.float32) - mid.astype(np.float32)).astype(bf)
    parts = [hi, mid, lo]
    rows = [parts[p] for _, n in K_RUNS for p in range(n)]
    key_stack = np.concatenate(rows + [np.ones((2, S), bf)])
    c, p = np.meshgrid(np.arange(128), np.arange(128), indexing="ij")
    corner = np.zeros((128, 128))
    corner[127, 0] = corner[0, 127] = NEG
    masks = np.stack([np.eye(128), np.where(c < p, NEG, 0), np.where(p <= c + 1, NEG, 0),
                      np.where(c > p, NEG, 0), np.where(c <= p + 1, NEG, 0), corner], 1).astype(bf)
    no_next = np.zeros((128, T), np.float32)
    no_next[127, T - 1] = NEG
    return {"tables": tables, "key_stack": key_stack, "masks": masks, "no_next": no_next,
            "eye": np.eye(128, dtype=np.float32)}


def program(nc, a, out):
    part = nc.dram_tensor("parts", (4, 3, 128, S), BF16, kind="Internal").ap()
    QU, RA, RB, KK = range(4)

    with ExitStack() as ctx:
        def sb(name, shape, dt, scope=ctx):
            return scope.enter_context(nc.sbuf_tensor(name, shape, dt))

        def sem(name):
            return ctx.enter_context(nc.semaphore(name))

        banks = ctx.enter_context(nc.psum_tensor("banks", [128, 8, 512], F32))

        masks = sb("masks_sb", [128, 6, 128], BF16)
        eye, m_ea, m_eb, m_pa, m_pb, m_corner = [masks[:, i, :] for i in range(6)]
        eye32 = sb("eye32", [128, 128], F32)
        nat = sb("nat", [128, T, 4 * C], F32)
        z = sb("z", [128, H, T], F32)
        nshift = sb("nshift", [128, H, T], F32)
        xb = sb("xb", [128, T, C], F32)
        no_next = sb("no_next_sb", [128, T], F32)

        in_q = sem("in_q")
        in_rest = sem("in_rest")
        proj_done = sem("proj_done")
        nat_done = sem("nat_done")
        nat_taken = sem("nat_taken")
        rot_terms = sem("rot_terms")
        whole = [sem(f"whole_{n}") for n in range(4)]
        hi_done = [sem(f"hi_{n}") for n in range(4)]
        res_done = [sem(f"res_{n}") for n in range(4)]
        mid_done = [sem(f"mid_{n}") for n in range(4)]
        lo_done = [sem(f"lo_{n}") for n in range(4)]
        parts_out = sem("parts_out")
        xb_in = sem("xb_in")
        xb_done = sem("xb_done")
        nat_q = sem("nat_q")
        nat_z = sem("nat_z")
        z_sum = sem("z_sum")
        z_done = sem("z_done")

        with ExitStack() as pre:
            xT = sb("xT_sb", [128, S + 1], F32, pre)
            wq = sb("wq", [128, C], F32, pre)
            wqs = sb("wqs", [128, C], F32, pre)
            wk = sb("wk", [128, C], F32, pre)
            w1 = sb("w1", [128, 2 * C], F32, pre)
            w2 = sb("w2", [128, 2 * C], F32, pre)
            bias = sb("bias", [128, 3], F32, pre)
            urow = sb("urow", [128, C], F32, pre)
            borow = sb("borow", [128, C], F32, pre)
            tab = sb("tab", [128, 4, S], F32, pre)
            val = sb("val", [128, 4, S + 1], F32, pre)
            term = sb("term", [128, 2, 2, 512], F32, pre)
            res = sb("res", [128, 4, 512], F32, pre)
            prt = sb("prt", [128, 4, 3, S + 1], BF16, pre)
            zprod = sb("zprod", [128, T, C], F32, pre)

            with nc.Block() as block:
                @block.sync
                def _(sp):
                    sp.dma_start(wq[:], a["L0_attn_Wq"]).then_inc(in_q, 16)
                    sp.dma_start(wqs[:], a["wq_swapped"]).then_inc(in_q, 16)
                    sp.dma_start(wk[:], a["L0_attn_Wk"]).then_inc(in_q, 16)
                    sp.dma_start(bias[:], a["head_bias"]).then_inc(in_q, 16)
                    sp.dma_start(xT[:, 0:1024], a["xT"][:, 0:1024]).then_inc(in_q, 16)
                    sp.dma_start(xT[:, 1024:S + 1], a["xT"][:, 1024:S + 1]).then_inc(in_q, 16)
                    for n in range(4):
                        src = a["tables"][n].rearrange("(o d) s -> o d s", o=1).to_broadcast([H, DK, S])
                        sp.dma_start(tab[:, n, :], src).then_inc(in_q, 16)
                    for n in range(4):
                        at = 1 if n == RB else 0
                        sp.wait_ge(lo_done[n], 5 if n == RB else 4)
                        sp.dma_start(part[n].rearrange("k p s -> p k s"),
                                     prt[:, n, :, at:at + S]).then_inc(parts_out, 16)
                    sp.wait_ge(parts_out, 64)

                @block.tensor
                def _(pe):
                    pe.wait_ge(in_q, 160)
                    for c in range(4):
                        if c >= 2:
                            pe.wait_ge(rot_terms, 2 * c - 2)
                            pe.wait_ge(whole[KK], c - 1)
                        for n, w in enumerate((wq, wqs, wk)):
                            pe.matmul(banks[:, 3 * (c % 2) + n, :], w[:], xT[:, 512 * c:512 * c + 512],
                                      start=True, stop=True).then_inc(proj_done, 1)
                    pe.wait_ge(in_rest, 128)
                    for t in range(T):
                        if t >= 2:
                            pe.wait_ge(nat_taken, t - 1)
                        pe.matmul(banks[:, 6 + t % 2, 0:256], xT[:, 128 * t:128 * t + 128], w1[:],
                                  start=True, stop=True)
                        pe.matmul(banks[:, 6 + t % 2, 256:512], xT[:, 128 * t + 1:128 * t + 129], w2[:],
                                  start=True, stop=True).then_inc(nat_done, 1)

                @block.scalar
                def _(act):
                    act.dma_start(w1[:, 0:C], a["L0_attn_Wq"]).then_inc(in_rest, 16)
                    act.dma_start(w1[:, C:2 * C], a["L0_attn_Wv"]).then_inc(in_rest, 16)
                    act.dma_start(w2[:, 0:C], a["L0_attn_Wk"]).then_inc(in_rest, 16)
                    act.dma_start(w2[:, C:2 * C], a["L0_attn_Wv"]).then_inc(in_rest, 16)
                    act.dma_start(masks[:], a["masks"]).then_inc(in_rest, 16)
                    act.dma_start(eye32[:], a["eye"]).then_inc(in_rest, 16)
                    act.dma_start(no_next[:], a["no_next"]).then_inc(in_rest, 16)
                    act.dma_start(urow[:], a["L0_attn_u"].rearrange("(o h) d -> o (h d)", o=1)
                                  .to_broadcast([128, C])).then_inc(in_rest, 16)
                    act.dma_start(xb[:], a["L0_attn_x"].rearrange("b (t p) c -> p (b t) c", p=128)) \
                        .then_inc(xb_in, 16)
                    act.dma_start(borow[:], a["L0_attn_bo"].rearrange("(o c) -> o c", o=1)
                                  .to_broadcast([128, C])).then_inc(xb_in, 16)
                    for c in range(4):
                        at = slice(512 * c, 512 * c + 512)
                        act.wait_ge(proj_done, 3 * c + 3)
                        act.copy(val[:, KK, at], banks[:, 3 * (c % 2) + 2, :]).then_inc(whole[KK], 1)
                        act.wait_ge(whole[KK], c + 1)
                        act.copy(prt[:, KK, 0, at], val[:, KK, at]).then_inc(hi_done[KK], 1)
                        for n in (QU, RA, RB):
                            act.wait_ge(whole[n], c + 1)
                            act.copy(prt[:, n, 0, at], val[:, n, at]).then_inc(hi_done[n], 1)
                        for n in (QU, RA, RB, KK):
                            act.wait_ge(res_done[n], c + 1)
                            act.copy(prt[:, n, 1, at], res[:, n, :]).then_inc(mid_done[n], 1)
                    for t in range(T):
                        act.wait_ge(nat_done, t + 1)
                        act.copy(nat[:, t, :], banks[:, 6 + t % 2, :]).then_inc(nat_taken, 1)

                @block.vector
                def _(dve):
                    dve.memset(prt[:, RB, :, S:S + 1], 0.0).then_inc(lo_done[RB], 1)
                    dve.wait_ge(in_q, 160)
                    for c in range(4):
                        at = slice(512 * c, 512 * c + 512)
                        q, qs = banks[:, 3 * (c % 2), :], banks[:, 3 * (c % 2) + 1, :]
                        dve.wait_ge(proj_done, 3 * c + 2)
                        if c >= 1:
                            dve.wait_ge(whole[RB], c)
                        dve.tensor_scalar(val[:, QU, at], q, bias[:, 0:1], None, ALU.add).then_inc(whole[QU], 1)
                        for n in range(2):
                            dve.scalar_tensor_tensor(term[:, n, 0, :], q, bias[:, 1:2], tab[:, 2 * n, at],
                                                     ALU.add, ALU.mult)
                            ins = dve.scalar_tensor_tensor(term[:, n, 1, :], qs, bias[:, 2:3],
                                                           tab[:, 2 * n + 1, at], ALU.add, ALU.mult)
                            ins.then_inc(rot_terms, 1)
                        for n in (KK, QU):
                            if c >= 1:
                                dve.wait_ge(lo_done[n], c)
                            dve.wait_ge(hi_done[n], c + 1)
                            dve.tensor_tensor(res[:, n, :], val[:, n, at], prt[:, n, 0, at],
                                              ALU.subtract).then_inc(res_done[n], 1)
                        for n in (QU, KK):
                            dve.wait_ge(mid_done[n], c + 1)
                            dve.tensor_tensor(prt[:, n, 2, at], res[:, n, :], prt[:, n, 1, at],
                                              ALU.subtract).then_inc(lo_done[n], 1)
                    dve.wait_ge(nat_z, 1)
                    dve.tensor_reduce(z[:].rearrange("p h t -> p t h"),
                                      zprod[:].rearrange("p t (h d) -> p t h d", h=H), AX.X, ALU.add) \
                        .then_inc(z_sum, 1)
                    dve.wait_ge(z_sum, 1)
                    dve.tensor_tensor(z[:], z[:], no_next[:].rearrange("p (o t) -> p o t", o=1)
                                      .to_broadcast([128, H, T]), ALU.add).then_inc(z_done, 1)

                @block.gpsimd
                def _(pool):
                    for c in range(4):
                        at = slice(512 * c, 512 * c + 512)
                        for i, n in enumerate((RA, RB)):
                            pool.wait_ge(rot_terms, 2 * c + i + 1)
                            pool.tensor_tensor(val[:, n, at], term[:, i, 0, :], term[:, i, 1, :],
                                               ALU.add).then_inc(whole[n], 1)
                        for n in (RA, RB):
                            if c >= 1:
                                pool.wait_ge(lo_done[n], c + (n == RB))
                            pool.wait_ge(hi_done[n], c + 1)
                            pool.tensor_tensor(res[:, n, :], val[:, n, at], prt[:, n, 0, at],
                                               ALU.subtract).then_inc(res_done[n], 1)
                        for n in (RA, RB):
                            pool.wait_ge(mid_done[n], c + 1)
                            pool.tensor_tensor(prt[:, n, 2, at], res[:, n, :], prt[:, n, 1, at],
                                               ALU.subtract).then_inc(lo_done[n], 1)
                    pool.wait_ge(in_rest, 128)
                    pool.wait_ge(nat_taken, T)
                    pool.tensor_tensor(nat[:, :, 0:C], nat[:, :, 0:C],
                                       urow[:].rearrange("p (o c) -> p o c", o=1).to_broadcast([128, T, C]),
                                       ALU.add).then_inc(nat_q, 1)
                    pool.wait_ge(nat_q, 1)
                    pool.tensor_tensor(zprod[:], nat[:, :, 0:C], nat[:, :, 2 * C:3 * C],
                                       ALU.mult).then_inc(nat_z, 1)
                    pool.wait_ge(xb_in, 32)
                    pool.tensor_tensor(xb[:], xb[:], borow[:].rearrange("p (o c) -> p o c", o=1)
                                       .to_broadcast([128, T, C]), ALU.add).then_inc(xb_done, 1)

        attention(nc, ctx, a, out, banks, masks, eye32, nat, z, nshift, xb, part)


def attention(nc, ctx, a, out, banks, masks, eye32, nat, z, nshift, xb, part):
    QU, RA, RB, KK = range(4)
    eye, m_ea, m_eb, m_pa, m_pb, m_corner = [masks[:, i, :] for i in range(6)]

    def sb(name, shape, dt, scope=ctx):
        return scope.enter_context(nc.sbuf_tensor(name, shape, dt))

    def sem(name):
        return ctx.enter_context(nc.semaphore(name))

    o_raw = sb("o_raw", [128, H, ECOLS], F32)

    def slot(n):
        return banks[:, 2 * (n % SLOTS):2 * (n % SLOTS) + 2, :].rearrange("p b c -> p (b c)")

    def piece(n):
        return banks[:, 4 + n % 3, :]

    pv_bank = banks[:, 7, :]

    stack_in = [sem(f"stack_in_{r}") for r in range(RING)]
    fixed_in = sem("fixed_in")
    shift_in = [sem(f"shift_in_{r}") for r in range(RING)]
    max_ready = sem("max_ready")
    max_taken = sem("max_taken")
    max_parts = sem("max_parts")
    score_ready = sem("score_ready")
    exp_done = sem("exp_done")
    pv_done = sem("pv_done")
    pv_free = sem("pv_free")
    v_zero = sem("v_zero")
    v_staged = sem("v_staged")

    def max_event(P, half):
        return 2 * P + half + 2 * max(0, (P - 1) // STEPS)

    def shift_event(h):
        return 2 * (STEPS * (h + 1) + (h < H - 1)) + 2 * h

    EVENTS = 2 * STEPS + 2

    with ExitStack() as att:
        qst = sb("qst", [128, RING, 2, S], BF16, att)
        kst = sb("kst", [128, RING, S], BF16, att)
        vst = sb("vst", [128, RING, T, 32], F32, att)
        et = sb("et", [128, RING, 4, ECOLS], F32, att)
        mx = sb("mx", [128, 3, T], F32, att)
        m1 = sb("m1", [128, 2, T], F32, att)
        nhl = sb("nhl", [128, 2, T], BF16, att)
        shT = sb("shT", [32, 128], BF16, att)

        def val(k, first, per_head):
            return first if k is None else first + k * (RING * per_head)

        def turn_val(k, first, per_turn):
            return first if k is None else first + k * per_turn

        def head(k, h):
            return h if k is None else h + k * RING

        with nc.Block() as block:
            @block.sync
            def _(sp):
                def load(k, h):
                    r = h % RING
                    hh = head(k, h)
                    rows = bass.ds(hh * DK, DK) if k is not None else slice(h * DK, h * DK + DK)
                    if h >= RING:
                        sp.wait_ge(score_ready, val(k, 4 * STEPS * (h - RING + 1), 4 * STEPS))
                    for v, kinds in enumerate(((QU, RA), (QU, RB))):
                        for i, kind in enumerate(kinds):
                            for first, p, n in Q_RUNS:
                                at = i * TYPE_ROWS + first * DK
                                src = part[kind, p, rows, :].rearrange("(o d) s -> o d s", o=1) \
                                    .to_broadcast([n, DK, S])
                                sp.dma_start(qst[at:at + n * DK, r, v, :], src).then_inc(stack_in[r], 16)
                    for first, n in K_RUNS:
                        at = first * DK
                        sp.dma_start(kst[at:at + n * DK, r, :], part[KK, 0:n, rows, :]) \
                            .then_inc(stack_in[r], 16)

                def shift(k, h):
                    r = h % RING
                    sp.wait_ge(max_taken, val(k, shift_event(h) + 2, EVENTS))
                    for v in range(2):
                        sp.dma_start(qst[SHIFT_ROW:SHIFT_ROW + 2, r, v, :], shT[:]).then_inc(shift_in[r], 16)

                for r in range(RING):
                    sp.dma_start(kst[TYPE_ROWS:STACK_ROWS, r, :], a["key_stack"]).then_inc(fixed_in, 16)
                load(None, 0)
                load(None, 1)
                shift(None, 0)
                load(None, 2)
                with sp.Fori(0, TURNS) as k:
                    for h in range(1, RING + 1):
                        shift(k, h)
                        load(k, h + 2)
                for h in range(RING * TURNS + 1, H):
                    shift(None, h)
                    if h + 2 < H:
                        load(None, h + 2)

            @block.tensor
            def _(pe):
                def max_pass(k, P, G):
                    h, t = P // STEPS, P % STEPS
                    r = h % RING
                    if t == 1 and h >= 1:
                        e = shift_event(h - 1)
                        pe.wait_ge(max_parts, val(k, 4 * h, 4))
                        pe.wait_ge(max_taken, val(k, e - 1, EVENTS))
                        pe.transpose(slot(e)[0:32, 0:64].bitcast(BF16), nhl[:].rearrange("p k t -> p (k t)"), eye) \
                            .then_inc(max_ready, 2)
                    if P >= ALL_STEPS and k is None:
                        return
                    if t == 0:
                        pe.wait_ge(stack_in[r], turn_val(k, 16 * STACK_DMAS * (h // RING + 1), 16 * STACK_DMAS))
                    for half in range(2):
                        e = max_event(P, half)
                        if e >= 2:
                            pe.wait_ge(max_taken, val(k, e - 1, EVENTS))
                        dst = slot(e)
                        for b in range(2):
                            o = dst[:, 512 * b:512 * b + 512]
                            j0 = 1024 * half + 512 * b
                            if t < T:
                                cut = min(max(128 * (t + 1) - j0, 0), 512)
                                q = slice(128 * t, 128 * t + 128)
                                todo = []
                                if cut > 0:
                                    todo.append((o[:, 0:cut], qst[0:SCORE_ROWS, r, 0, q],
                                                 kst[0:SCORE_ROWS, r, j0:j0 + cut]))
                                if cut < 512:
                                    todo.append((o[:, cut:512], qst[0:SCORE_ROWS, r, 1, q],
                                                 kst[0:SCORE_ROWS, r, j0 + cut:j0 + 512]))
                                d = 128 * t - j0
                                if 0 <= d < 512:
                                    todo.append((o[:, d:d + 128], m_pa, eye))
                                if 0 <= d + 128 < 512:
                                    todo.append((o[:, d + 128:d + 129], m_corner, eye[:, 0:1]))
                            else:
                                todo = []
                                for x in range(4):
                                    q = slice(j0 + 128 * x, j0 + 128 * x + 128)
                                    todo.append((o[:, 128 * x:128 * x + 128], qst[0:SCORE_ROWS, r, 1, q],
                                                 kst[0:SCORE_ROWS, r, q]))
                                todo.append((o.rearrange("p (n c) -> p n c", n=4), m_pb, four_eyes))
                            for n, (dst_ap, lhsT, rhs) in enumerate(todo):
                                ins = pe.matmul(dst_ap, lhsT, rhs, start=(n == 0), stop=(n == len(todo) - 1),
                                                skip_group_check=True)
                        ins.then_inc(max_ready, 1)

                four_eyes = eye.rearrange("p (o c) -> p o c", o=1).to_broadcast([128, 4, 128])

                def scores(k, G):
                    h, jb = G // STEPS, G % STEPS
                    r = h % RING
                    if jb == 0:
                        pe.wait_ge(shift_in[r], turn_val(k, 32 * (h // RING + 1), 32))
                    for x in range(4):
                        n = 4 * G + x
                        if n >= 3:
                            pe.wait_ge(exp_done, val(k, n - 2, 4 * STEPS))
                        o = piece(n)
                        i0 = 512 * x
                        if jb < T:
                            cut = min(max(128 * jb - i0, 0), 512)
                            lhsT = kst[0:STACK_ROWS, r, 128 * jb:128 * jb + 128]
                            todo = []
                            if cut > 0:
                                todo.append((o[:, 0:cut], lhsT, qst[0:STACK_ROWS, r, 1, i0:i0 + cut]))
                            if cut < 512:
                                todo.append((o[:, cut:512], lhsT, qst[0:STACK_ROWS, r, 0, i0 + cut:i0 + 512]))
                            d = 128 * jb - i0
                            if 0 <= d < 512:
                                todo.append((o[:, d:d + 128], m_ea, eye))
                            if 0 < d <= 512:
                                todo.append((o[:, d - 1:d], m_corner, eye[:, 127:128]))
                        else:
                            todo = []
                            for y in range(4):
                                q = slice(i0 + 128 * y, i0 + 128 * y + 128)
                                todo.append((o[:, 128 * y:128 * y + 128], kst[0:STACK_ROWS, r, q],
                                             qst[0:STACK_ROWS, r, 1, q]))
                            todo.append((o.rearrange("p (n c) -> p n c", n=4), m_eb, four_eyes))
                        for m, (dst_ap, lhsT, rhs) in enumerate(todo):
                            ins = pe.matmul(dst_ap, lhsT, rhs, start=(m == 0), stop=(m == len(todo) - 1),
                                            skip_group_check=True)
                        ins.then_inc(score_ready, 1)

                def values(k, G):
                    h, jb = G // STEPS, G % STEPS
                    r = h % RING
                    g = G % RING
                    pe.wait_ge(exp_done, val(k, 4 * G + 4, 4 * STEPS))
                    if jb == 0:
                        pe.wait_ge(v_staged, val(k, h + 1, 1))
                        pe.wait_ge(pv_free, val(k, h + 1, 1))
                    if jb < T:
                        for x in range(4):
                            ins = pe.matmul(pv_bank[32 * x:32 * x + 32, :], vst[:, r, jb, :], et[:, g, x, :],
                                            start=(jb == 0), stop=False, skip_group_check=True)
                    else:
                        for y in range(4):
                            for x in range(4):
                                c = slice(128 * y, 128 * y + 128)
                                ins = pe.matmul(pv_bank[32 * x:32 * x + 32, c], vst[:, r, 4 * x + y, :],
                                                et[:, g, x, c], start=False, stop=(y == 3),
                                                skip_group_check=True)
                    ins.then_inc(pv_done, 1)

                def step(k, G):
                    if G + LEAD < ALL_STEPS + 2 or k is not None:
                        max_pass(k, G + LEAD, G)
                    scores(k, G)
                    if G >= 1:
                        values(k, G - 1)

                pe.wait_ge(fixed_in, 16 * RING)
                for P in range(LEAD):
                    max_pass(None, P, None)
                max_pass(None, LEAD, 0)
                scores(None, 0)
                with pe.Fori(0, TURNS) as k:
                    for G in range(1, BODY + 1):
                        step(k, G)
                for G in range(BODY * TURNS + 1, ALL_STEPS):
                    step(None, G)
                values(None, ALL_STEPS - 1)

            @block.scalar
            def _(act):
                def step(k, G):
                    g = G % RING
                    if G >= RING or k is not None:
                        act.wait_ge(pv_done, val(k, G - RING + 1, STEPS))
                    for x in range(4):
                        n = 4 * G + x
                        act.wait_ge(score_ready, val(k, n + 1, 4 * STEPS))
                        act.activation(et[:, g, x, :], piece(n), ACT.Exp, scale=SCALE).then_inc(exp_done, 1)

                for G in range(RING):
                    step(None, G)
                with act.Fori(0, TURNS) as k:
                    for G in range(RING, BODY + RING):
                        step(k, G)
                for G in range(BODY * TURNS + RING, ALL_STEPS):
                    step(None, G)

            @block.vector
            def _(dve):
                def shift_parts(k, h):
                    hh = slice(h, h + 1) if k is None else bass.ds(head(k, h), 1)
                    zh = z[:, hh, :].rearrange("p o t -> p (o t)")
                    nh = nshift[:, hh, :].rearrange("p o t -> p (o t)")
                    dve.wait_ge(max_taken, val(k, max_event(STEPS * h + STEPS - 1, 1) + 1, EVENTS))
                    dve.tensor_reduce(m1[:, 0, :], mx[:].rearrange("p k t -> p t k"), AX.X, ALU.max) \
                        .then_inc(max_parts, 1)
                    dve.wait_ge(max_parts, val(k, 4 * h + 1, 4))
                    dve.tensor_tensor(m1[:, 1, :], m1[:, 0, :], zh, ALU.max).then_inc(max_parts, 1)
                    dve.wait_ge(max_parts, val(k, 4 * h + 2, 4))
                    dve.tensor_scalar(nhl[:, 0, :], m1[:, 1, :], -1.0, None, ALU.mult).then_inc(max_parts, 1)
                    dve.wait_ge(max_parts, val(k, 4 * h + 3, 4))
                    dve.scalar_tensor_tensor(nhl[:, 1, :], m1[:, 1, :], -1.0, nhl[:, 0, :], ALU.mult,
                                             ALU.subtract).then_inc(max_parts, 1)
                    dve.wait_ge(max_parts, val(k, 4 * h + 4, 4))
                    dve.tensor_tensor(nh, nhl[:, 0, :], nhl[:, 1, :], ALU.add)

                def max_step(k, P):
                    h, t = P // STEPS, P % STEPS
                    if t == 1 and h >= 1:
                        e = shift_event(h - 1)
                        dve.wait_ge(max_ready, val(k, e + 2, EVENTS))
                        if h >= 2:
                            dve.wait_ge(shift_in[(h - 2) % RING], turn_val(k, 32 * ((h - 2) // RING + 1), 32))
                        dve.tensor_copy(shT[:], slot(e)[0:32, 0:64].bitcast(BF16)).then_inc(max_taken, 2)
                    if P >= ALL_STEPS and k is None:
                        return
                    for half in range(2):
                        e = max_event(P, half)
                        dve.wait_ge(max_ready, val(k, e + 1, EVENTS))
                        if t < T:
                            dve.tensor_reduce(mx[:, half, t:t + 1], slot(e), AX.X, ALU.max).then_inc(max_taken, 1)
                        else:
                            dve.tensor_reduce(mx[:, 2, 8 * half:8 * half + 8],
                                              slot(e).rearrange("p (n c) -> p n c", c=128),
                                              AX.X, ALU.max).then_inc(max_taken, 1)
                    if t == T:
                        shift_parts(k, h)

                def step(k, G):
                    if G % STEPS == 1 and G > STEPS:
                        h = G // STEPS - 1
                        hh = slice(h, h + 1) if k is None else bass.ds(head(k, h), 1)
                        dve.wait_ge(pv_done, val(k, STEPS * (h + 1), STEPS))
                        dve.tensor_copy(o_raw[:, hh, :].rearrange("p o c -> p (o c)"), pv_bank) \
                            .then_inc(pv_free, 1)
                    if G + LEAD < ALL_STEPS + 2 or k is not None:
                        max_step(k, G + LEAD)

                dve.sem_inc(pv_free, 1)
                for P in range(LEAD):
                    max_step(None, P)
                step(None, 0)
                step(None, 1)
                with dve.Fori(0, TURNS) as k:
                    for G in range(2, BODY + 2):
                        step(k, G)
                for G in range(BODY * TURNS + 2, ALL_STEPS):
                    step(None, G)
                dve.wait_ge(pv_done, ALL_STEPS)
                dve.tensor_copy(o_raw[:, H - 1, :], pv_bank).then_inc(pv_free, 1)

            @block.gpsimd
            def _(pool):
                pool.memset(vst[:], 0.0).then_inc(v_zero, 1)
                pool.wait_ge(v_zero, 1)
                pool.memset(vst[:, :, :, DK:DK + 1], 1.0).then_inc(v_zero, 1)
                pool.wait_ge(v_zero, 2)

                def stage(k, h):
                    if h >= RING:
                        pool.wait_ge(pv_done, val(k, STEPS * (h - RING + 1), STEPS))
                    at = slice(C + h * DK, C + h * DK + DK) if k is None else \
                        bass.ds(head(k, h) * DK + C, DK)
                    pool.tensor_copy(vst[:, h % RING, :, 0:DK], nat[:, :, at]).then_inc(v_staged, 1)

                for h in range(RING):
                    stage(None, h)
                with pool.Fori(0, TURNS) as k:
                    for h in range(RING, 2 * RING):
                        stage(k, h)
                stage(None, H - 1)

    finish(nc, ctx, a, out, banks, eye32, nat, z, nshift, xb, o_raw)


MIDS = [0.25, 0.75, 1.25, 1.75, 2.5, 3.5, 5.0]
BLK = 16
FIRST = 4
CH = [(0, 128), (128, 128), (256, 96)]


def finish(nc, ctx, a, out, banks, eye32, nat, z, nshift, xb, o_raw):
    def sb(name, shape, dt):
        return ctx.enter_context(nc.sbuf_tensor(name, shape, dt))

    def sem(name):
        return ctx.enter_context(nc.semaphore(name))

    W_COLS = 2 * 3 * 128 + INNER
    wo = sb("wo", [128, C], F32)
    w_raw = sb("w_raw", [128, W_COLS], F32)
    w_q = sb("w_q", [128, W_COLS], F32)
    wguT = sb("wguT", [128, 2, 384], F32)
    wdT = sb("wdT", [128, 3, 128], F32)
    w_abs = sb("w_abs", [128, W_COLS], F32)
    w_cnt = sb("w_cnt", [128, W_COLS], F32)
    w_sgn = sb("w_sgn", [128, W_COLS], F32)
    w_mag = sb("w_mag", [128, W_COLS], F32)
    w_max = sb("w_max", [128, W_COLS // BLK], F32)
    w_scl = sb("w_scl", [128, W_COLS // BLK], F32)
    o_nat = sb("o_nat", [128, T, H, DK + 1], F32)
    ez = sb("ez", [128, H, T], F32)
    zs = sb("zs", [128, H, T], F32)
    zv = sb("zv", [128, T, H, DK], F32)
    rden = sb("rden", [128, T, H], F32)
    att = sb("att", [128, 2, C], F32)
    attT = sb("attT", [128, 2, C], F32)
    y = sb("y", [128, 2, C], F32)
    moment = sb("moment", [128, 2, 3], F32)
    square = sb("square", [128, C], F32)
    rstd = sb("rstd", [128, 2, 1], F32)
    x1 = sb("x1", [128, 2, C], F32)
    xq = sb("xq", [128, 2, C], F32)
    xqT = sb("xqT", [128, 2, C], F32)
    eg = sb("eg", [128, 2, INNER], F32)
    hid = sb("hid", [128, 2, INNER], F32)
    hq = sb("hq", [128, 2, INNER], F32)
    hqT = sb("hqT", [128, 2, 3, 128], F32)
    yo = sb("yo", [128, 2, C], F32)
    sgn_x = sb("sgn_x", [128, 2, C], F32)
    mag_x = sb("mag_x", [128, 2, C], F32)
    sgn_h = sb("sgn_h", [128, 2, INNER], F32)
    mag_h = sb("mag_h", [128, 2, INNER], F32)
    t_abs = sb("t_abs", [128, INNER], F32)
    t_cnt = sb("t_cnt", [128, INNER], F32)
    t_max = sb("t_max", [128, INNER // BLK], F32)
    t_scl = sb("t_scl", [128, INNER // BLK], F32)

    w_in = sem("w_in")
    w_pad = sem("w_pad")
    w_signs = sem("w_signs")
    w_quant = sem("w_quant")
    w_T = sem("w_T")
    w_copied = sem("w_copied")
    o_T = sem("o_T")
    o_even = sem("o_even")
    o_odd = sem("o_odd")
    zs_done = sem("zs_done")
    ez_done = sem("ez_done")
    att_done = sem("att_done")
    att_T = sem("att_T")
    att_copied = sem("att_copied")
    wo_done = sem("wo_done")
    wo_taken = sem("wo_taken")
    x1_done = sem("x1_done")
    sgn_x_done = sem("sgn_x_done")
    xq_done = sem("xq_done")
    xq_T = sem("xq_T")
    xq_copied = sem("xq_copied")
    gu_done = sem("gu_done")
    eg_done = sem("eg_done")
    hid_done = sem("hid_done")
    sgn_h_done = sem("sgn_h_done")
    hq_done = sem("hq_done")
    hq_T = sem("hq_T")
    hq_copied = sem("hq_copied")
    down_done = sem("down_done")
    down_taken = sem("down_taken")
    yo_done = sem("yo_done")
    stored = [sem("stored_0"), sem("stored_1")]
    chain = sem("dve_chain")
    var_done = sem("var_done")
    half_set = sem("half_set")
    rstd_done = sem("rstd_done")
    half = sb("half", [128, 1], F32)
    veps = sb("veps", [128, 2, 1], F32)

    def tv(k, first, per_tile=1):
        return first if k is None else first + k * (2 * per_tile)

    x_out = out.rearrange("b (t p) c -> (b t) p c", p=128)

    def run(eng, A, B, Cc):
        def step(k, s):
            if k is not None or s >= 2:
                Cc(k, s - 2)
            if k is not None or s < T:
                A(k, s)
            if k is not None or 1 <= s <= T:
                B(k, s - 1)
        for s in range(FIRST):
            step(None, s)
        with eng.Fori(0, (T - FIRST) // 2) as k:
            for s in (FIRST, FIRST + 1):
                step(k, s)
        step(None, T)
        step(None, T + 1)

    with nc.Block() as block:
        @block.sync
        def _(sp):
            sp.dma_start(wo[:], a["L0_attn_Wo"]).then_inc(w_in, 16)
            sp.wait_ge(w_pad, 1)
            for m, w in enumerate(("L0_ffn_w_gate", "L0_ffn_w_up")):
                for c, (r0, n) in enumerate(CH):
                    at = (3 * m + c) * 128
                    sp.dma_start(w_raw[0:n, at:at + 128], a[w][r0:r0 + n, :]).then_inc(w_in, 16)
            sp.dma_start(w_raw[:, 768:W_COLS], a["L0_ffn_w_down"]).then_inc(w_in, 16)

            def nothing(k, t):
                pass

            def store(k, t):
                b = t % 2
                sp.wait_ge(yo_done, tv(k, t + 1))
                dst = x_out[t] if k is None else x_out[bass.ds(t + k * 2, 1)].rearrange("o p c -> (o p) c")
                sp.dma_start(dst, yo[:, b, :]).then_inc(stored[b], 16)

            run(sp, nothing, nothing, store)
            for b in range(2):
                sp.wait_ge(stored[b], 16 * (T // 2))

        @block.tensor
        def _(pe):
            for h in range(H):
                if h >= 4:
                    pe.wait_ge(o_even if h % 2 == 0 else o_odd, h // 2 - 1)
                for c in range(4):
                    ins = pe.transpose(banks[:, h % 4, 128 * c:128 * c + 128],
                                       o_raw[:, h, 128 * c:128 * c + 128], eye32[:])
                ins.then_inc(o_T, 1)
            pe.wait_ge(w_quant, 1)
            for m in range(2):
                for c, (r0, n) in enumerate(CH):
                    at = (3 * m + c) * 128
                    ins = pe.transpose(banks[:, 4 + m, 128 * c:128 * c + 128], w_q[:, at:at + 128], eye32[:])
            for c, (r0, n) in enumerate(CH):
                ins = pe.transpose(banks[0:n, 6, 128 * c:128 * c + 128], w_q[:, 768 + r0:768 + r0 + n], eye32[:])
            ins.then_inc(w_T, 1)
            pe.wait_ge(w_copied, 3)
            pe.wait_ge(o_even, H // 2)
            pe.wait_ge(o_odd, H // 2)
            pe.wait_ge(w_in, 16)

            def A(k, t):
                b = t % 2
                pe.wait_ge(att_done, tv(k, t + 1))
                if k is not None or t >= 1:
                    pe.wait_ge(xq_copied, tv(k, t))
                pe.transpose(banks[:, 4, 0:128], att[:, b, :], eye32[:]).then_inc(att_T, 1)
                pe.wait_ge(att_copied, tv(k, t + 1))
                if k is not None or t >= 1:
                    pe.wait_ge(wo_taken, tv(k, t))
                pe.matmul(banks[:, 5, 0:128], attT[:, b, :], wo[:], start=True, stop=True).then_inc(wo_done, 1)
                pe.wait_ge(xq_done, tv(k, t + 1))
                pe.transpose(banks[:, 4, 0:128], xq[:, b, :], eye32[:]).then_inc(xq_T, 1)

            def B(k, t):
                b = t % 2
                pe.wait_ge(xq_copied, tv(k, t + 1))
                if k is not None or t >= 2:
                    pe.wait_ge(hid_done, tv(k, t - 1))
                    pe.wait_ge(eg_done, tv(k, t - 1))
                for m in range(2):
                    ins = pe.matmul(banks[:, 2 * b + m, 0:INNER], xqT[:, b, :], wguT[:, m, 0:INNER],
                                    start=True, stop=True)
                ins.then_inc(gu_done, 1)
                pe.wait_ge(hq_done, tv(k, t + 1))
                if k is not None or t >= 1:
                    pe.wait_ge(hq_copied, tv(k, t))
                for c, (r0, n) in enumerate(CH):
                    ins = pe.transpose(banks[0:n, 6, 128 * c:128 * c + 128], hq[:, b, r0:r0 + n], eye32[:])
                ins.then_inc(hq_T, 1)

            def Cc(k, t):
                b = t % 2
                pe.wait_ge(hq_copied, tv(k, t + 1))
                if k is not None or t >= 1:
                    pe.wait_ge(down_taken, tv(k, t))
                for c, (r0, n) in enumerate(CH):
                    ins = pe.matmul(banks[:, 7, 0:128], hqT[0:n, b, c, :], wdT[0:n, c, :],
                                    start=(c == 0), stop=(c == 2))
                ins.then_inc(down_done, 1)

            run(pe, A, B, Cc)

        def o_view(h):
            return banks[:, h % 4, :].rearrange("p (c q d) -> p q c d", c=4, q=4)[:, :, :, 0:DK + 1]

        def o_dst(h):
            return o_nat[:, :, h, :].rearrange("p (q c) d -> p q c d", q=4)

        @block.scalar
        def _(act):
            act.wait_ge(zs_done, 1)
            act.activation(ez[:], zs[:], ACT.Exp, scale=SCALE).then_inc(ez_done, 1)
            act.wait_ge(w_in, 128)
            act.activation(w_mag[:], w_raw[:], ACT.Abs)
            act.activation(w_sgn[:], w_raw[:], ACT.Sign).then_inc(w_signs, 1)
            for h in range(0, H, 2):
                act.wait_ge(o_T, h + 1)
                act.copy(o_dst(h), o_view(h)).then_inc(o_even, 1)
            act.wait_ge(w_T, 1)
            act.copy(wguT[:, 0, :], banks[:, 4, 0:384]).then_inc(w_copied, 1)
            act.copy(wguT[:, 1, :], banks[:, 5, 0:384]).then_inc(w_copied, 1)
            act.copy(wdT[:, 0:2, :], banks[:, 6, 0:256].rearrange("p (c n) -> p c n", c=2))
            act.copy(wdT[0:96, 2, :], banks[0:96, 6, 256:384]).then_inc(w_copied, 1)

            def A(k, t):
                b = t % 2
                act.wait_ge(att_T, tv(k, t + 1))
                act.copy(attT[:, b, :], banks[:, 4, 0:128]).then_inc(att_copied, 1)
                act.wait_ge(x1_done, tv(k, t + 1))
                if k is not None or t >= 2:
                    act.wait_ge(xq_done, tv(k, t - 1))
                x1t = x1[:, b, :]
                act.activation(mag_x[:, b, :], x1t, ACT.Abs)
                act.activation(sgn_x[:, b, :], x1t, ACT.Sign).then_inc(sgn_x_done, 1)
                act.wait_ge(xq_T, tv(k, t + 1))
                if k is not None or t >= 2:
                    act.wait_ge(gu_done, tv(k, t - 1))
                act.copy(xqT[:, b, :], banks[:, 4, 0:128]).then_inc(xq_copied, 1)

            def B(k, t):
                b = t % 2
                act.wait_ge(gu_done, tv(k, t + 1))
                if k is not None or t >= 2:
                    act.wait_ge(hid_done, tv(k, t - 1))
                act.activation(eg[:, b, :], banks[:, 2 * b, 0:INNER], ACT.Silu).then_inc(eg_done, 1)
                act.wait_ge(hid_done, tv(k, t + 1))
                if k is not None or t >= 2:
                    act.wait_ge(hq_done, tv(k, t - 1))
                act.activation(mag_h[:, b, :], hid[:, b, :], ACT.Abs)
                act.activation(sgn_h[:, b, :], hid[:, b, :], ACT.Sign).then_inc(sgn_h_done, 1)
                act.wait_ge(hq_T, tv(k, t + 1))
                if k is not None or t >= 2:
                    act.wait_ge(down_done, tv(k, t - 1))
                act.copy(hqT[:, b, 0:2, :], banks[:, 6, 0:256].rearrange("p (c n) -> p c n", c=2))
                act.copy(hqT[0:96, b, 2, :], banks[0:96, 6, 256:384]).then_inc(hq_copied, 1)

            def Cc(k, t):
                pass

            run(act, A, B, Cc)

        @block.gpsimd
        def _(pool):
            pool.memset(half[:], -0.5).then_inc(half_set, 1)
            pool.wait_ge(half_set, 1)
            count = [0]

            def norm(k, b):
                count[0] += 1
                n = count[0]
                def c(v):
                    return v if k is None else v + k * 4
                pool.wait_ge(var_done, c(n))
                pool.tensor_tensor(rstd[:, b, :], veps[:, b, :], half[:], ALU.pow).then_inc(rstd_done, 1)

            def step(k, s):
                if k is not None or s < T:
                    norm(k, s % 2)
                if k is not None or s >= 2:
                    norm(k, s % 2)

            for s in range(FIRST):
                step(None, s)
            with pool.Fori(0, (T - FIRST) // 2) as k:
                for s in (FIRST, FIRST + 1):
                    step(k, s)
            count[0] += 4 * ((T - FIRST) // 2 - 1)
            step(None, T)
            step(None, T + 1)

        @block.vector
        def _(dve):
            done = [0]

            def link(k, ins, per_turn=0):
                done[0] += 1
                ins.then_inc(chain, 1)
                dve.wait_ge(chain, done[0] if k is None else k * per_turn + done[0])

            def fp4(k, per, dst, src, sgn, mag, width, ab, cnt, mxb, scl, wait_sign, ready):
                nb = width // BLK
                def blocks(ap):
                    return ap.rearrange("p (n b) -> p n b", b=BLK)
                def wide(ap):
                    return ap.rearrange("p (n o) -> p n o", o=1).to_broadcast([128, nb, BLK])
                link(k, dve.tensor_reduce(mxb, blocks(src), AX.X, ALU.max, apply_absolute_value=True), per)
                link(k, dve.tensor_scalar(scl, mxb, 1.0 / 6.0, 1e-12, ALU.mult, ALU.max), per)
                link(k, dve.reciprocal(mxb, scl), per)
                wait_sign()
                link(k, dve.tensor_tensor(blocks(ab), blocks(mag), wide(mxb), ALU.mult), per)
                link(k, dve.tensor_scalar(cnt, ab, MIDS[6], 2.0, ALU.is_gt, ALU.mult), per)
                link(k, dve.scalar_tensor_tensor(cnt, ab, MIDS[5], cnt, ALU.is_gt, ALU.add), per)
                link(k, dve.scalar_tensor_tensor(cnt, ab, MIDS[4], cnt, ALU.is_gt, ALU.add), per)
                link(k, dve.tensor_scalar(cnt, cnt, 2.0, None, ALU.mult), per)
                for m in MIDS[3::-1]:
                    link(k, dve.scalar_tensor_tensor(cnt, ab, m, cnt, ALU.is_gt, ALU.add), per)
                link(k, dve.scalar_tensor_tensor(cnt, cnt, 0.5, sgn, ALU.mult, ALU.mult), per)
                dve.tensor_tensor(blocks(dst), blocks(cnt), wide(scl), ALU.mult).then_inc(ready, 1)

            dve.memset(w_raw[:], 0.0).then_inc(w_pad, 1)
            dve.tensor_tensor(zs[:], z[:], nshift[:], ALU.add).then_inc(zs_done, 1)
            dve.wait_ge(w_in, 128)
            fp4(None, 0, w_q[:], w_raw[:], w_sgn[:], w_mag[:], W_COLS, w_abs[:], w_cnt[:], w_max[:], w_scl[:],
                lambda: dve.wait_ge(w_signs, 1), w_quant)
            for h in range(1, H, 2):
                dve.wait_ge(o_T, h + 1)
                dve.tensor_copy(o_dst(h), o_view(h)).then_inc(o_odd, 1)
            dve.wait_ge(ez_done, 1)
            ezt = ez[:].rearrange("p h t -> p t h")
            ez4 = ez[:].rearrange("p h (t o) -> p t h o", o=1).to_broadcast([128, T, H, DK])
            vn = nat[:, :, 3 * C:4 * C].rearrange("p t (h d) -> p t h d", h=H)
            dve.wait_ge(o_odd, H // 2)
            dve.wait_ge(o_even, H // 2)
            link(None, dve.tensor_tensor(zv[:], vn, ez4, ALU.mult))
            link(None, dve.tensor_tensor(zv[:], zv[:], o_nat[:, :, :, 0:DK], ALU.add))
            link(None, dve.tensor_tensor(rden[:], o_nat[:, :, :, DK:DK + 1].rearrange("p t h o -> p t (h o)"),
                                         ezt, ALU.add))
            link(None, dve.reciprocal(rden[:], rden[:]))

            norm_step = [0]

            def norm_count(k, n):
                return n if k is None else n + k * 4

            def norm(k, per, product, residual, dst, b, taken, ready):
                dve.scalar_tensor_tensor(y[:, b, :], product, 1.0, residual, ALU.mult, ALU.add,
                                         accum_out=moment[:, b, 0:1]).then_inc(taken[0], 1)
                dve.wait_ge(*taken)
                link(k, dve.tensor_scalar(moment[:, b, 1:2], moment[:, b, 0:1], 1.0 / C, None, ALU.mult), per)
                link(k, dve.tensor_scalar(y[:, b, :], y[:, b, :], moment[:, b, 1:2], None, ALU.subtract), per)
                link(k, dve.scalar_tensor_tensor(square[:], y[:, b, :], 1.0, y[:, b, :], ALU.mult, ALU.mult,
                                                 accum_out=moment[:, b, 2:3]), per)
                dve.tensor_scalar(veps[:, b, :], moment[:, b, 2:3], 1.0 / C, LN_EPS, ALU.mult, ALU.add) \
                    .then_inc(var_done, 1)
                norm_step[0] += 1
                dve.wait_ge(rstd_done, norm_count(k, norm_step[0]))
                dve.tensor_scalar(dst, y[:, b, :], rstd[:, b, :], None, ALU.mult).then_inc(ready, 1)

            def A(k, t):
                b = t % 2
                per = PER
                tt = slice(t, t + 1) if k is None else bass.ds(t + k * 2, 1)
                if k is not None or t >= 2:
                    dve.wait_ge(att_T, tv(k, t - 1))
                dve.tensor_tensor(att[:, b, :].rearrange("p (o h d) -> p o h d", o=1, h=H), zv[:, tt, :, :],
                                  rden[:, tt, :].rearrange("p o (h e) -> p o h e", e=1)
                                  .to_broadcast([128, 1, H, DK]), ALU.mult).then_inc(att_done, 1)
                dve.wait_ge(wo_done, tv(k, t + 1))
                x1t = x1[:, b, :]
                norm(k, per, banks[:, 5, 0:128], xb[:, tt, :].rearrange("p o c -> p (o c)"), x1t, b,
                     (wo_taken, tv(k, t + 1)), x1_done)
                dve.wait_ge(x1_done, tv(k, t + 1))
                fp4(k, per, xq[:, b, :], x1t, sgn_x[:, b, :], mag_x[:, b, :], C, t_abs[:, 0:C], t_cnt[:, 0:C],
                    t_max[:, 0:C // BLK], t_scl[:, 0:C // BLK],
                    lambda: dve.wait_ge(sgn_x_done, tv(k, t + 1)), xq_done)

            def B(k, t):
                b = t % 2
                dve.wait_ge(eg_done, tv(k, t + 1))
                dve.tensor_tensor(hid[:, b, :], eg[:, b, :], banks[:, 2 * b + 1, 0:INNER], ALU.mult) \
                    .then_inc(hid_done, 1)
                dve.wait_ge(hid_done, tv(k, t + 1))
                fp4(k, PER, hq[:, b, :], hid[:, b, :], sgn_h[:, b, :], mag_h[:, b, :], INNER, t_abs[:], t_cnt[:],
                    t_max[:], t_scl[:], lambda: dve.wait_ge(sgn_h_done, tv(k, t + 1)), hq_done)

            def Cc(k, t):
                b = t % 2
                x1t = x1[:, b, :]
                dve.wait_ge(down_done, tv(k, t + 1))
                if k is not None or t >= 2:
                    dve.wait_ge(stored[b], tv(k, 16 * (t // 2), 8))
                norm(k, PER, banks[:, 7, 0:128], x1t, yo[:, b, :], b, (down_taken, tv(k, t + 1)), yo_done)

            FP4_LINKS = 13
            PER = 2 * (3 + FP4_LINKS + FP4_LINKS + 3)

            def steps():
                def step(k, s):
                    if k is not None or s >= 2:
                        Cc(k, s - 2)
                    if k is not None or s < T:
                        A(k, s)
                    if k is not None or 1 <= s <= T:
                        B(k, s - 1)
                for s in range(FIRST):
                    step(None, s)
                before = done[0]
                with dve.Fori(0, (T - FIRST) // 2) as k:
                    for s in (FIRST, FIRST + 1):
                        step(k, s)
                assert done[0] - before == PER, (done[0] - before, PER)
                done[0] = before + PER * ((T - FIRST) // 2)
                norm_step[0] += 4 * ((T - FIRST) // 2 - 1)
                step(None, T)
                step(None, T + 1)
            steps()


_INS = ["L0_attn_x", "L0_attn_Wq", "L0_attn_Wk", "L0_attn_Wv", "L0_attn_u", "L0_attn_v", "L0_attn_Wo",
        "L0_attn_bo", "L0_ffn_w_gate", "L0_ffn_w_up", "L0_ffn_w_down"]


def kernel(**inputs):
    import concourse.bacc as bacc
    from concourse.bass_utils import run_bass_kernel_spmd

    arrays = {n: np.ascontiguousarray(inputs[n]) for n in _INS}
    xt = np.zeros((C, S + 1), arrays["L0_attn_x"].dtype)
    xt[:, :S] = arrays["L0_attn_x"][0].T
    swap = np.arange(C).reshape(H, 2, DK // 2)[:, ::-1].reshape(C)
    v = arrays["L0_attn_v"].reshape(C)
    arrays["xT"] = xt
    arrays["wq_swapped"] = np.ascontiguousarray(arrays["L0_attn_Wq"][:, swap])
    arrays["head_bias"] = np.ascontiguousarray(np.stack([arrays["L0_attn_u"].reshape(C), v, v[swap]], 1))
    arrays.update(constants())

    nc = bacc.Bacc("TRN2", target_bir_lowering=False, num_devices=1)
    aps = {n: nc.dram_tensor(n, x.shape, mybir.dt.from_np(x.dtype), kind="ExternalInput").ap()
           for n, x in arrays.items()}
    out = nc.dram_tensor("out", (1, S, C), F32, kind="ExternalOutput").ap()
    program(nc, aps, out)
    got = run_bass_kernel_spmd(nc, [arrays], core_ids=[0])
    return got.results[0]["out"]
```
